# Optimizing a Trainium2 kernel written in Bass

```python
import numpy as np
import jax
import jax.numpy as jnp

def _softmax(x, axis=-1):
    return jax.nn.softmax(x, axis=axis)

def _gelu(x):
    return jax.nn.gelu(x, approximate=True)

def _silu(x):
    return jax.nn.silu(x)

def _sigmoid(x):
    return jax.nn.sigmoid(x)

def _layernorm(x, axis=-1, eps=1e-05):
    m = jnp.mean(x, axis=axis, keepdims=True)
    v = jnp.var(x, axis=axis, keepdims=True)
    return (x - m) / jnp.sqrt(v + eps)

def _scatter_add(tgt, idx, src, axis=0):
    return tgt.at[idx].add(src)

def _segment_sum(src, seg, n):
    return jax.ops.segment_sum(src, seg, n)
kernel_name = 'mk_macaron_d1_jaxref_r8_be6764'

def setup_inputs(seed: int=0):
    np.random.seed(seed)
    _w = jnp.asarray

    def _L0_attn_setup():
        import jax, jax.numpy as jnp
        import numpy as np
        NUM_HEADS = 16
        HEAD_DIM = 64
        NEG_INF = -1000000000.0

        def rotary_embedding(x, seq_len, head_dim):
            positions = jnp.arange(seq_len)
            dim_pairs = jnp.arange(0, head_dim, 2)
            freqs = 1.0 / 10000.0 ** (dim_pairs / head_dim)
            angles = positions[:, None] * freqs[None, :]
            cos = jnp.cos(angles)[:, None, :]
            sin = jnp.sin(angles)[:, None, :]
            x1 = x[..., ::2]
            x2 = x[..., 1::2]
            out1 = x1 * cos - x2 * sin
            out2 = x1 * sin + x2 * cos
            return jnp.stack([out1, out2], axis=-1).reshape(x.shape)
        key = jax.random.key(seed)
        k1, k2, k3 = jax.random.split(key, 3)
        batch, seq_len, embed_dim = (2, 256, 128)
        x = jax.random.normal(k1, (batch, seq_len, embed_dim), dtype=jnp.float32)
        W_qkv = jax.random.normal(k2, (embed_dim, 3 * NUM_HEADS * HEAD_DIM), dtype=jnp.float32) * 0.02
        W_out = jax.random.normal(k3, (NUM_HEADS * HEAD_DIM, embed_dim), dtype=jnp.float32) * 0.02
        return {'x': x, 'W_qkv': W_qkv, 'W_out': W_out}
    _L0_attn_in = _L0_attn_setup()

    def _L0_ffn_setup():
        import jax, jax.numpy as jnp
        import numpy as np
        N_EXPERTS = 32
        TOP_K = 8
        N_GROUP = 4
        TOPK_GROUP = 2
        ROUTED_SCALING = 2.5

        def _gate(x, gate_w, gate_bias):
            T, E = (x.shape[0], gate_w.shape[0])
            logits = jnp.einsum('th,eh->te', x, gate_w)
            scores = jax.nn.sigmoid(logits)
            scores_choice = scores + gate_bias[None, :]
            grp = scores_choice.reshape(T, N_GROUP, E // N_GROUP)
            top2, _ = jax.lax.top_k(grp, 2)
            group_scores = top2.sum(-1)
            _, grp_idx = jax.lax.top_k(group_scores, TOPK_GROUP)
            group_mask = jax.nn.one_hot(grp_idx, N_GROUP, dtype=scores.dtype).sum(1)
            expert_mask = jnp.repeat(group_mask, E // N_GROUP, axis=1)
            masked = jnp.where(expert_mask > 0, scores_choice, 0.0)
            _, topk_idx = jax.lax.top_k(masked, TOP_K)
            topk_w = jnp.take_along_axis(scores, topk_idx, axis=1)
            topk_w = topk_w / (topk_w.sum(-1, keepdims=True) + 1e-20)
            topk_w = topk_w * ROUTED_SCALING
            return (topk_idx, topk_w)

        def _mlp(x, wg, wu, wd):
            return jnp.einsum('...i,hi->...h', jax.nn.silu(jnp.einsum('...h,ih->...i', x, wg)) * jnp.einsum('...h,ih->...i', x, wu), wd)
        key = jax.random.key(seed)
        ks = jax.random.split(key, 9)
        B, S, H, I = (2, 64, 128, 64)
        w = 0.02
        return {'hidden_states': jax.random.normal(ks[0], (B, S, H), jnp.float32), 'gate_w': jax.random.normal(ks[1], (N_EXPERTS, H), jnp.float32) * w, 'gate_bias': jax.random.normal(ks[2], (N_EXPERTS,), jnp.float32) * w, 'expert_gate': jax.random.normal(ks[3], (N_EXPERTS, I, H), jnp.float32) * w, 'expert_up': jax.random.normal(ks[4], (N_EXPERTS, I, H), jnp.float32) * w, 'expert_down': jax.random.normal(ks[5], (N_EXPERTS, H, I), jnp.float32) * w, 'shared_gate': jax.random.normal(ks[6], (2 * I, H), jnp.float32) * w, 'shared_up': jax.random.normal(ks[7], (2 * I, H), jnp.float32) * w, 'shared_down': jax.random.normal(ks[8], (H, 2 * I), jnp.float32) * w}
    _L0_ffn_in = _L0_ffn_setup()
    _d = {'L0_attn_x': _L0_attn_in['x'], 'L0_attn_W_qkv': _L0_attn_in['W_qkv'], 'L0_attn_W_out': _L0_attn_in['W_out'], 'L0_ffn_gate_w': _L0_ffn_in['gate_w'], 'L0_ffn_gate_bias': _L0_ffn_in['gate_bias'], 'L0_ffn_expert_gate': _L0_ffn_in['expert_gate'], 'L0_ffn_expert_up': _L0_ffn_in['expert_up'], 'L0_ffn_expert_down': _L0_ffn_in['expert_down'], 'L0_ffn_shared_gate': _L0_ffn_in['shared_gate'], 'L0_ffn_shared_up': _L0_ffn_in['shared_up'], 'L0_ffn_shared_down': _L0_ffn_in['shared_down']}
    _x0 = _d['L0_attn_x']
    _d['L0_attn_x'] = jax.random.normal(jax.random.fold_in(jax.random.key(seed), 1), (16, 512, 128), dtype=_x0.dtype)
    del _x0
    return _d

def reference(L0_attn_x, L0_attn_W_qkv, L0_attn_W_out, L0_ffn_gate_w, L0_ffn_gate_bias, L0_ffn_expert_gate, L0_ffn_expert_up, L0_ffn_expert_down, L0_ffn_shared_gate, L0_ffn_shared_up, L0_ffn_shared_down):

    def _L0_attn_ref(x, W_qkv, W_out):
        import jax, jax.numpy as jnp
        import numpy as np
        NUM_HEADS = 16
        HEAD_DIM = 64
        NEG_INF = -1000000000.0

        def rotary_embedding(x, seq_len, head_dim):
            positions = jnp.arange(seq_len)
            dim_pairs = jnp.arange(0, head_dim, 2)
            freqs = 1.0 / 10000.0 ** (dim_pairs / head_dim)
            angles = positions[:, None] * freqs[None, :]
            cos = jnp.cos(angles)[:, None, :]
            sin = jnp.sin(angles)[:, None, :]
            x1 = x[..., ::2]
            x2 = x[..., 1::2]
            out1 = x1 * cos - x2 * sin
            out2 = x1 * sin + x2 * cos
            return jnp.stack([out1, out2], axis=-1).reshape(x.shape)
        batch, seq_len, embed_dim = x.shape
        qkv = jnp.einsum('bse,ef->bsf', x, W_qkv)
        qkv = qkv.reshape(batch, seq_len, 3, NUM_HEADS, HEAD_DIM)
        q, k, v = (qkv[:, :, 0], qkv[:, :, 1], qkv[:, :, 2])
        q = rotary_embedding(q, seq_len, HEAD_DIM)
        k = rotary_embedding(k, seq_len, HEAD_DIM)
        scale = 1.0 / jnp.sqrt(jnp.asarray(HEAD_DIM, dtype=x.dtype))
        scores = jnp.einsum('bqhd,bkhd->bhqk', q, k) * scale
        mask = jnp.tril(jnp.ones((seq_len, seq_len), dtype=bool))[None, None, :, :]
        scores = jnp.where(mask, scores, NEG_INF)
        weights = jax.nn.softmax(scores, axis=-1)
        out = jnp.einsum('bhqk,bkhd->bqhd', weights, v)
        out = out.reshape(batch, seq_len, NUM_HEADS * HEAD_DIM)
        return jnp.einsum('bsf,fe->bse', out, W_out)

    def _L0_ffn_ref(hidden_states, gate_w, gate_bias, expert_gate, expert_up, expert_down, shared_gate, shared_up, shared_down):
        import jax, jax.numpy as jnp
        import numpy as np
        N_EXPERTS = 32
        TOP_K = 8
        N_GROUP = 4
        TOPK_GROUP = 2
        ROUTED_SCALING = 2.5

        def _gate(x, gate_w, gate_bias):
            T, E = (x.shape[0], gate_w.shape[0])
            logits = jnp.einsum('th,eh->te', x, gate_w)
            scores = jax.nn.sigmoid(logits)
            scores_choice = scores + gate_bias[None, :]
            grp = scores_choice.reshape(T, N_GROUP, E // N_GROUP)
            top2, _ = jax.lax.top_k(grp, 2)
            group_scores = top2.sum(-1)
            _, grp_idx = jax.lax.top_k(group_scores, TOPK_GROUP)
            group_mask = jax.nn.one_hot(grp_idx, N_GROUP, dtype=scores.dtype).sum(1)
            expert_mask = jnp.repeat(group_mask, E // N_GROUP, axis=1)
            masked = jnp.where(expert_mask > 0, scores_choice, 0.0)
            _, topk_idx = jax.lax.top_k(masked, TOP_K)
            topk_w = jnp.take_along_axis(scores, topk_idx, axis=1)
            topk_w = topk_w / (topk_w.sum(-1, keepdims=True) + 1e-20)
            topk_w = topk_w * ROUTED_SCALING
            return (topk_idx, topk_w)

        def _mlp(x, wg, wu, wd):
            return jnp.einsum('...i,hi->...h', jax.nn.silu(jnp.einsum('...h,ih->...i', x, wg)) * jnp.einsum('...h,ih->...i', x, wu), wd)
        orig_shape = hidden_states.shape
        H = orig_shape[-1]
        residuals = hidden_states
        x = hidden_states.reshape(-1, H)
        topk_idx, topk_w = _gate(x, gate_w, gate_bias)
        g = jnp.einsum('th,eih->eti', x, expert_gate)
        u = jnp.einsum('th,eih->eti', x, expert_up)
        outs = jnp.einsum('eti,ehi->eth', jax.nn.silu(g) * u, expert_down)
        outs_t = jnp.transpose(outs, (1, 0, 2))
        gathered = jnp.take_along_axis(outs_t, topk_idx[:, :, None], axis=1)
        final = (gathered * topk_w[:, :, None]).sum(1)
        shared = _mlp(residuals, shared_gate, shared_up, shared_down)
        return final.reshape(orig_shape) + shared
    x = L0_attn_x
    x = x + 0.5 * _L0_ffn_ref(_layernorm(x, axis=-1), L0_ffn_gate_w, L0_ffn_gate_bias, L0_ffn_expert_gate, L0_ffn_expert_up, L0_ffn_expert_down, L0_ffn_shared_gate, L0_ffn_shared_up, L0_ffn_shared_down)
    x = x + _L0_attn_ref(_layernorm(x, axis=-1), L0_attn_W_qkv, L0_attn_W_out)
    x = x + 0.5 * _L0_ffn_ref(_layernorm(x, axis=-1), L0_ffn_gate_w, L0_ffn_gate_bias, L0_ffn_expert_gate, L0_ffn_expert_up, L0_ffn_expert_down, L0_ffn_shared_gate, L0_ffn_shared_up, L0_ffn_shared_down)
    return x

_drawn_inputs = setup_inputs


def setup_inputs(seed=0):
    import zlib

    import numpy as np

    out = dict(_drawn_inputs(seed))
    spreads = {}
    factors = {'L0_attn_W_qkv': 3.389,
     'L0_attn_W_out': 3.385,
     'L0_ffn_gate_w': 8.0,
     'L0_ffn_gate_bias': 8.0,
     'L0_ffn_expert_gate': 8.0,
     'L0_ffn_expert_up': 8.0,
     'L0_ffn_expert_down': 8.0,
     'L0_ffn_shared_gate': 8.0,
     'L0_ffn_shared_up': 8.0,
     'L0_ffn_shared_down': 8.0}
    for name, (base, spread) in spreads.items():
        noise = np.random.default_rng([zlib.crc32(name.encode()), seed]).standard_normal(out[name].shape)
        drawn = base * np.exp(spread * noise) if base else spread * noise
        out[name] = jnp.asarray(drawn.astype(out[name].dtype))
    for name, factor in factors.items():
        out[name] = (out[name] * factor).astype(out[name].dtype)
    return out
```

```python
import concourse.bass as bass
import concourse.mybir as mybir
import numpy as np
from contextlib import ExitStack

F32 = mybir.dt.float32
F32R = mybir.dt.float32r
BF16 = mybir.dt.bfloat16
ALU = mybir.AluOpType
ACT = mybir.ActivationFunctionType
AX = mybir.AxisListType

P = 128
T = 512
SUB = T // P
NT = 16
SLOTS = NT + 3
E = 32
I = 64
PAIRS = E // 2
STEPS = PAIRS + 1
GROUPS = 4
GE = E // GROUPS
KEEP_GROUPS = 2
TOPK = 8
SPLIT = 3
HEADS = 16
D = 64
HP = HEADS // 2
HEAD_ROWS = 32
EPS = 1e-5
SCALING = 2.5
NEG = -3.0e38
MASKED = -1e30


def constants():
    c = {}
    c["ident"] = np.eye(P, dtype=np.float32)
    c["center"] = (np.eye(P) - 1.0 / P).astype(np.float32)
    sel = np.zeros((SPLIT * E, PAIRS, 2, I), np.float32)
    for r in range(SPLIT * E):
        sel[r, (r % E) // 2, (r % E) % 2, :] = 1.0
    c["sel_expert"] = sel.reshape(SPLIT * E, PAIRS * P)
    sel = np.zeros((SPLIT * HEAD_ROWS, HP, 2, D), np.float32)
    for r in range(SPLIT * HEAD_ROWS):
        if r % HEAD_ROWS < HEADS:
            sel[r, r % HEAD_ROWS // 2, r % HEAD_ROWS % 2, :] = 1.0
    c["sel_head"] = sel.reshape(SPLIT * HEAD_ROWS, HP * P)
    before = np.zeros((SUB, GROUPS, GROUPS), np.float32)
    for j in range(GROUPS):
        before[:, j, :j] = 1.0
    c["before"] = np.broadcast_to(before.reshape(1, -1), (P, SUB * GROUPS * GROUPS)).copy()
    c["mask"] = np.where(np.tril(np.ones((P, P), bool)), 0.0, MASKED).astype(np.float32)
    pairs = np.arange(0, D, 2).astype(np.float32)
    freqs = (np.float32(1.0) / np.power(np.float32(10000.0), pairs / np.float32(D))).astype(np.float32)
    angles = (np.arange(T).astype(np.float32)[:, None] * freqs[None, :]).astype(np.float32)
    row = np.arange(P) % D
    cos = np.cos(angles).astype(np.float32)[:, row // 2].T
    sin = np.sin(angles).astype(np.float32)[:, row // 2].T * np.where(row % 2, 1.0, -1.0)[:, None]
    scale = 1.0 / 8.0
    c["rot_q"] = np.concatenate([cos * scale, sin * scale], 1).astype(np.float32)
    c["rot_k"] = np.concatenate([cos, sin], 1).astype(np.float32)
    return {k: np.ascontiguousarray(v) for k, v in c.items()}


def tile(buf, slot):
    return buf[:, bass.ds(slot * T, T)]


def ffn_phase(nc, ph, g, w_dram, x_dram, out_dram):
    post = out_dram is None
    INITS = 2 if x_dram is not None else 1
    PIECE = STEPS * P // 2
    PIECES = 6
    STAGES = 6
    NORMS = 2 if post else 1
    with ExitStack() as ctx:
        def sb(name, shape, dt=F32):
            return ctx.enter_context(nc.sbuf_tensor(f"{ph}_{name}", shape, dt))

        def sem(name):
            return ctx.enter_context(nc.semaphore(f"{ph}_{name}"))

        x = g["x"]
        w_gate, w_up, w_down = ([sb(f"{n}_{part}", [P, STEPS * P], F32R) for part in ("hi", "lo")]
                                for n in ("w_gate", "w_up", "w_down"))
        stage = [sb(f"stage{i}", [P, PIECE]) for i in range(STAGES)]
        ident, ident16, ones, center = g["ident"], g["ident16"], g["ones"], g["center"]

        xn = sb("xn", [P, T])
        xn_hi, xn_lo = ([sb(f"xn_{part}{i}", [P, T], F32R) for i in range(2)] for part in ("hi", "lo"))
        w_t = [sb(f"w_t{i}", [SPLIT * E, T], BF16) for i in range(2)]
        act_g = [sb(f"act_g{i}", [P, T]) for i in range(2)]
        prod = [sb(f"prod{i}", [P, T]) for i in range(2)]
        hidden = [sb(f"hidden{i}", [P, T]) for i in range(2)]
        hidden_hi, hidden_lo = ([sb(f"hidden_{part}{i}", [P, T], F32R) for i in range(2)] for part in ("hi", "lo"))
        xn_out = [sb(f"xn_out{i}", [P, T]) for i in range(2)] if post else None
        cen = sb("cen", [P, T])
        sq = sb("sq", [P, T])
        var = sb("var", [P, SUB])
        rstd = sb("rstd", [P, SUB])
        diag = sb("diag", [P, SUB, P])
        NE = SUB * E
        NG = SUB * GROUPS
        zero_fix = sb("zero_fix", [P, NE])
        logit = sb("logit", [P, NE])
        inv_logit = sb("inv_logit", [P, NE])
        silu_logit = sb("silu_logit", [P, NE])
        score = sb("score", [P, NE])
        choice = sb("choice", [P, NE])
        hi4, lo4 = sb("hi4", [P, NG, 4]), sb("lo4", [P, NG, 4])
        hi2, lo2 = sb("hi2", [P, NG, 2]), sb("lo2", [P, NG, 2])
        m2, n2 = sb("m2", [P, NG, 2]), sb("n2", [P, NG, 2])
        hi1, lo1 = sb("hi1", [P, NG]), sb("lo1", [P, NG])
        m1, n1 = sb("m1", [P, NG]), sb("n1", [P, NG])
        g_score = sb("g_score", [P, NG])
        g_gt, g_eq, g_tie = (sb(n, [P, SUB, GROUPS, GROUPS]) for n in ("g_gt", "g_eq", "g_tie"))
        g_beaten = sb("g_beaten", [P, SUB, GROUPS, GROUPS])
        g_count, g_keep = sb("g_count", [P, NG]), sb("g_keep", [P, NG])
        masked = sb("masked", [P, NE])
        top8 = sb("top8", [P, SUB, TOPK])
        left = sb("left", [P, NE])
        picked = sb("picked", [P, NE])
        w_raw = sb("w_raw", [P, NE])
        w_sum, w_sum1, w_inv, w_inv1 = (sb(n, [P, SUB]) for n in ("w_sum", "w_sum1", "w_inv", "w_inv1"))
        w_norm, w_rest = sb("w_norm", [P, NE]), sb("w_rest", [P, NE])
        w_split = sb("w_split", [P, SUB, SPLIT * E], BF16)

        def pb(name):
            return ctx.enter_context(nc.psum_tensor(f"{ph}_{name}", [P, T], F32))

        gate_ps = [pb(f"gate_ps{i}") for i in range(2)]
        up_ps = [pb(f"up_ps{i}") for i in range(2)]
        wbc_ps = [pb(f"wbc_ps{i}") for i in range(2)]
        out_ps = pb("out_ps")
        misc_ps = pb("misc_ps")
        w_t_ps = misc_ps[0:SPLIT * E, :].bitcast(BF16)

        loaded = [sem(f"loaded{i}") for i in range(2)]
        staged = [sem(f"staged{i}") for i in range(PIECES)]
        piece_hi, piece_lo = sem("piece_hi"), sem("piece_lo")
        init = sem("init")
        gate_up, up_up, wbc_up = sem("gate_up"), sem("up_up"), sem("wbc_up")
        silu_done = sem("silu_done")
        up_used = sem("up_used")
        hidden_up = sem("hidden_up")
        hi_up, lo_up = sem("hi_up"), sem("lo_up")
        xn_hi_up, xn_lo_up = sem("xn_hi_up"), sem("xn_lo_up")
        down_done = sem("down_done")
        tile_done = sem("tile_done")
        centered_ps, centered = sem("centered_ps"), sem("centered")
        var_ps, var_taken = sem("var_ps"), sem("var_taken")
        rstd_up, diag_up, rstd_ps = sem("rstd_up"), sem("diag_up"), sem("rstd_ps")
        normed = sem("normed")
        logits_ps, logits_taken, inv_up = sem("logits_ps"), sem("logits_taken"), sem("inv_up")
        silu_logit_up = sem("silu_logit_up")
        choice_up, keep_up, masked_up, raw_up = sem("choice_up"), sem("keep_up"), sem("masked_up"), sem("raw_up")
        split_up, w_t_in_ps, w_t_up = sem("split_up"), sem("w_t_in_ps"), sem("w_t_up")
        dve_chain, pool_chain = sem("dve_chain"), sem("pool_chain")
        stored = sem("stored")
        xn_stored = [sem(f"xn_stored{i}") for i in range(2)] if post else None

        start_at_1 = [silu_done, up_used, down_done] + (xn_stored if post else [])

        def post_no(i):
            return i * NORMS + 2

        def pre_no(i):
            return i * NORMS + 1 + NORMS

        def wait_products(eng, i, p):
            if p == 2:
                eng.wait_ge(hidden_up, i * STEPS + p + 1)
            else:
                eng.wait_ge(up_used, i * PAIRS + (p if p < 2 else p - 1) + 1)

        with nc.Block() as block:

            @block.sync
            def _(sp):
                if x_dram is not None:
                    for t in range(2):
                        sp.dma_start(tile(x, t + 1), x_dram[:, t * T:(t + 1) * T]).then_inc(loaded[t], 16)
                for c in range(PIECES):
                    at = c % 2 * PIECE
                    sp.dma_start(stage[c][:], w_dram[c // 2][:, at:at + PIECE]).then_inc(staged[c], 16)
                if x_dram is not None:
                    for t in range(2, NT + 2):
                        sp.wait_ge(loaded[t % 2], 16 * (t // 2))
                        at = t % NT * T
                        sp.dma_start(tile(x, t + 1), x_dram[:, at:at + T]).then_inc(loaded[t % 2], 16)
                if post:
                    with sp.Fori(0, NT // 2) as it:
                        for par in range(2):
                            i = it * 2 + par
                            sp.wait_ge(normed, post_no(i) + 1)
                            sp.dma_start(g["xn_dram"][:, bass.ds(i * T, T)], xn_out[par][:]).then_inc(xn_stored[par], 16)
                    sp.wait_ge(normed, post_no(NT) + 1)
                    sp.dma_start(g["xn_dram"][:, NT * T:(NT + 1) * T], xn_out[0][:]).then_inc(xn_stored[0], 16)
                    sp.wait_ge(xn_stored[0], 16 * (NT // 2 + 1) + 1)
                    sp.wait_ge(xn_stored[1], 16 * (NT // 2) + 1)
                if out_dram is not None:
                    with sp.Fori(0, NT) as t:
                        sp.wait_ge(tile_done, t + 2)
                        sp.dma_start(out_dram[:, bass.ds(t * T, T)], tile(x, t + 1)).then_inc(stored, 16)
                    sp.wait_ge(stored, 16 * NT)

            @block.tensor
            def _(pe):
                def mm3(out, w, cols, x, start=True, stop=True):
                    nc.tensor.matmul(out, w[0][:, cols], x[0][:], start=start, stop=False, skip_group_check=True)
                    nc.tensor.matmul(out, w[0][:, cols], x[1][:], start=False, stop=False, skip_group_check=True)
                    return nc.tensor.matmul(out, w[1][:, cols], x[0][:], start=False, stop=stop, skip_group_check=True)

                def center_mm(slot):
                    nc.tensor.matmul(misc_ps[:], center[:], tile(x, slot), start=True, stop=True).then_inc(centered_ps, 1)

                def var_mm(n):
                    pe.wait_ge(centered, 2 * n + 2)
                    for j in range(SUB):
                        last = nc.tensor.matmul(misc_ps[:, j:j + 1], sq[:, j * P:(j + 1) * P], g["mean_col"][:],
                                                start=True, stop=True)
                    last.then_inc(var_ps, 1)

                def rstd_mm(n):
                    pe.wait_ge(diag_up, n + 1)
                    pe.wait_ge(var_taken, n + 1)
                    nc.tensor.matmul(misc_ps[:], ones[:], diag[:].rearrange("p j t -> p (j t)"),
                                     start=True, stop=True).then_inc(rstd_ps, 1)

                def logits_mm(n):
                    for j in range(SUB):
                        last = nc.tensor.matmul(misc_ps[:, j * E:(j + 1) * E], xn[:, j * P:(j + 1) * P],
                                                g["w_router"][:], start=True, stop=True)
                    last.then_inc(logits_ps, 1)

                def w_t_mm(n):
                    pe.wait_ge(split_up, n + 1)
                    for j in range(SUB):
                        last = nc.tensor.transpose(w_t_ps[:, j * P:(j + 1) * P], w_split[:, j, :], ident16[:])
                    last.then_inc(w_t_in_ps, 1)

                def down_mm(k, q, b, i):
                    pe.wait_ge(hi_up, k + 1)
                    pe.wait_ge(lo_up, k + 1)
                    if q == 0:
                        pe.wait_ge(tile_done, i + 1)
                    mm3(out_ps[:], w_down, slice(q * P, (q + 1) * P), (hidden_hi[b], hidden_lo[b]),
                        start=(q == 0), stop=(q == STEPS - 1)).then_inc(down_done, 1)

                def turn(it, par):
                    i = it * 2 + par
                    for p in range(STEPS):
                        k = i * STEPS + p
                        b = (STEPS * par + p) % 2
                        pe.wait_ge(silu_done, k + 1)
                        if p == 0:
                            pe.wait_ge(xn_hi_up, i + 1)
                            pe.wait_ge(xn_lo_up, i + 1)
                        xs = (xn_hi[par], xn_lo[par])
                        cols = slice(p * P, (p + 1) * P)
                        mm3(gate_ps[b][:], w_gate, cols, xs).then_inc(gate_up, 1)
                        wait_products(pe, i, p)
                        mm3(up_ps[b][:], w_up, cols, xs).then_inc(up_up, 1)
                        if p > 0:
                            pe.wait_ge(hidden_up, k + 1)
                            nc.tensor.matmul(wbc_ps[p % 2][:], g["sel_expert"][:, (p - 1) * P:p * P], w_t[par][:],
                                             start=True, stop=True).then_inc(wbc_up, 1)
                        down_mm(k, (p - 2) % STEPS, b, i)
                        if p == 0:
                            pe.wait_ge(w_t_up, i + 1)
                            logits_mm(i + 1)
                        if post and p == 2:
                            pe.wait_ge(logits_taken, i + 2)
                            center_mm(i)
                        if post and p == 4:
                            var_mm(post_no(i))
                        if post and p == 8:
                            rstd_mm(post_no(i))
                        if p == 9:
                            pe.wait_ge(logits_taken, i + 2)
                            pe.wait_ge(normed, pre_no(i))
                            if x_dram is not None:
                                pe.wait_ge(loaded[par], 16 * (it + 2))
                            center_mm(i + 3)
                        if p == 12:
                            var_mm(pre_no(i))
                        if p == 15:
                            rstd_mm(pre_no(i))
                        if p == 16:
                            pe.wait_ge(normed, pre_no(i) + 1)
                            w_t_mm(i + 1)

                pe.wait_ge(init, INITS)
                if x_dram is not None:
                    pe.wait_ge(loaded[0], 16)
                pe.wait_ge(g["consts"], g["n_consts"])
                pe.wait_ge(g["cast"], g["n_cast"])
                center_mm(1)
                var_mm(0)
                rstd_mm(0)
                pe.wait_ge(normed, 1)
                logits_mm(0)
                if x_dram is not None:
                    pe.wait_ge(loaded[1], 16)
                pe.wait_ge(logits_taken, 1)
                center_mm(2)
                var_mm(1)
                rstd_mm(1)
                pe.wait_ge(normed, 2)
                w_t_mm(0)
                pe.wait_ge(piece_hi, PIECES)
                pe.wait_ge(piece_lo, PIECES)
                with pe.Fori(0, NT // 2) as it:
                    for par in range(2):
                        turn(it, par)
                for q in (STEPS - 2, STEPS - 1):
                    k = NT * STEPS + q - STEPS + 2
                    down_mm(k, q, k % 2, NT)
                if post:
                    pe.wait_ge(w_t_up, NT + 1)
                    pe.wait_ge(tile_done, NT + 1)
                    center_mm(NT)
                    var_mm(post_no(NT))
                    rstd_mm(post_no(NT))

            @block.scalar
            def _(act):
                def center(n):
                    act.wait_ge(centered_ps, n + 1)
                    nc.scalar.copy(cen[:], misc_ps[:]).then_inc(centered, 1)
                    nc.scalar.activation(sq[:], misc_ps[:], ACT.Square).then_inc(centered, 1)

                def hidden_high(m, b):
                    act.wait_ge(hidden_up, m + 1)
                    act.wait_ge(down_done, m - 1 + 1)
                    nc.scalar.copy(hidden_hi[b][:], hidden[b][:]).then_inc(hi_up, 1)

                def xn_high(par, count):
                    act.wait_ge(normed, count)
                    nc.scalar.copy(xn_hi[par][:], xn[:]).then_inc(xn_hi_up, 1)

                def silu_of_logits(n):
                    act.wait_ge(logits_taken, n + 1)
                    nc.scalar.activation(silu_logit[:], logit[:], ACT.Silu).then_inc(silu_logit_up, 1)

                def take_w_t(n, par):
                    act.wait_ge(w_t_in_ps, n + 1)
                    nc.scalar.copy(w_t[par][:], w_t_ps[:, 0:T]).then_inc(w_t_up, 1)

                def turn(it, par):
                    i = it * 2 + par
                    for p in range(STEPS):
                        k = i * STEPS + p
                        b = (STEPS * par + p) % 2
                        if p == 0:
                            take_w_t(i, par)
                        act.wait_ge(gate_up, k + 1)
                        wait_products(act, i, p)
                        nc.scalar.activation(act_g[b][:], gate_ps[b][:], ACT.Silu).then_inc(silu_done, 1)
                        hidden_high(k + 1, 1 - b)
                        if p == 1:
                            xn_high(1 - par, i * NORMS + 2)
                        if p == 2:
                            silu_of_logits(i + 1)
                        if post and p == 3:
                            center(post_no(i))
                        if p == 10:
                            center(pre_no(i))

                act.wait_ge(g["consts"], g["n_consts"])
                nc.scalar.activation(silu_logit[:, 0:1], g["mean_col"][:], ACT.Silu).then_inc(silu_done, 1)
                def weights_high(c):
                    act.wait_ge(staged[c], 16)
                    nc.scalar.copy((w_gate, w_up, w_down)[c // 2][0][:, c % 2 * PIECE:(c % 2 + 1) * PIECE],
                                   stage[c][:]).then_inc(piece_hi, 1)

                center(0)
                weights_high(0)
                weights_high(1)
                xn_high(0, 1)
                silu_of_logits(0)
                weights_high(2)
                center(1)
                for c in range(3, PIECES):
                    weights_high(c)
                with act.Fori(0, NT // 2) as it:
                    for par in range(2):
                        turn(it, par)
                hidden_high(NT * STEPS + 1, (NT * STEPS + 1) % 2)
                take_w_t(NT, 0)
                if post:
                    center(post_no(NT))

            @block.gpsimd
            def _(pool):
                def rstd_step(n):
                    pool.wait_ge(var_taken, n + 1)
                    nc.gpsimd.tensor_tensor(rstd[:], var[:], g["minus_half"][:], ALU.pow).then_inc(rstd_up, 1)

                def diag_step(n):
                    pool.wait_ge(rstd_up, n + 1)
                    nc.gpsimd.tensor_tensor(diag[:], ident[:].unsqueeze(1).broadcast_to([P, SUB, P]),
                                            rstd[:].unsqueeze(2).broadcast_to([P, SUB, P]), ALU.mult).then_inc(diag_up, 1)

                def hidden_low(m, b):
                    pool.wait_ge(hi_up, m + 1)
                    pool.wait_ge(down_done, m - 1 + 1)
                    nc.gpsimd.tensor_tensor(hidden_lo[b][:], hidden[b][:], hidden_hi[b][:].bitcast(F32),
                                            ALU.subtract).then_inc(lo_up, 1)

                def xn_low(n, par):
                    pool.wait_ge(xn_hi_up, n + 1)
                    nc.gpsimd.tensor_tensor(xn_lo[par][:], xn[:], xn_hi[par][:].bitcast(F32),
                                            ALU.subtract).then_inc(xn_lo_up, 1)

                def scores(n):
                    pool.wait_ge(silu_logit_up, n + 1)
                    pool.wait_ge(inv_up, n + 1)
                    nc.gpsimd.tensor_tensor(score[:], silu_logit[:], inv_logit[:], ALU.mult).then_inc(pool_chain, 1)
                    pool.wait_ge(pool_chain, n + 1)
                    nc.gpsimd.tensor_tensor(choice[:].rearrange("p (j e) -> p j e", e=E),
                                            score[:].rearrange("p (j e) -> p j e", e=E),
                                            g["bias"][:].unsqueeze(1).broadcast_to([P, SUB, E]),
                                            ALU.add).then_inc(choice_up, 1)

                def mask_groups(n):
                    pool.wait_ge(keep_up, n + 1)
                    nc.gpsimd.tensor_tensor(masked[:].rearrange("p (g e) -> p g e", e=GE),
                                            choice[:].rearrange("p (g e) -> p g e", e=GE),
                                            g_keep[:].unsqueeze(2).broadcast_to([P, NG, GE]),
                                            ALU.mult).then_inc(masked_up, 1)

                for count in start_at_1:
                    nc.gpsimd.sem_inc(count, 1)
                nc.gpsimd.memset(hidden_hi[0][:].bitcast(F32), 0.0).then_inc(hi_up, 1)
                nc.gpsimd.memset(hidden_lo[0][:].bitcast(F32), 0.0).then_inc(lo_up, 1)
                nc.gpsimd.memset(hidden[1][:], 0.0).then_inc(hidden_up, 1)
                pool.wait_ge(g["consts"], g["n_consts"])
                rstd_step(0)
                diag_step(0)
                xn_low(0, 0)
                scores(0)
                mask_groups(0)
                rstd_step(1)
                diag_step(1)
                with pool.Fori(0, NT // 2) as it:
                    for par in range(2):
                        i = it * 2 + par
                        for p in range(STEPS):
                            b = (STEPS * par + p) % 2
                            hidden_low(i * STEPS + p + 1, 1 - b)
                            if p == 1:
                                xn_low(i + 1, 1 - par)
                            if p == 3:
                                scores(i + 1)
                            if post and p == 5:
                                rstd_step(post_no(i))
                            if post and p == 6:
                                diag_step(post_no(i))
                            if p == 8:
                                mask_groups(i + 1)
                            if p == 12:
                                rstd_step(pre_no(i))
                            if p == 13:
                                diag_step(pre_no(i))
                hidden_low(NT * STEPS + 1, (NT * STEPS + 1) % 2)
                if post:
                    rstd_step(post_no(NT))
                    diag_step(post_no(NT))

            @block.vector
            def _(dve):
                LINKS = 20

                def link(ins, n, c):
                    ins.then_inc(dve_chain, 1)
                    dve.wait_ge(dve_chain, n * LINKS + c)

                def take_var(n):
                    dve.wait_ge(var_ps, n + 1)
                    nc.vector.tensor_scalar_add(var[:], misc_ps[:, 0:SUB], EPS).then_inc(var_taken, 1)

                def scale(n, dst):
                    dve.wait_ge(rstd_ps, n + 1)
                    dve.wait_ge(centered, 2 * n + 2)
                    nc.vector.tensor_mul(dst, cen[:], misc_ps[:]).then_inc(normed, 1)

                def xn_free(n):
                    dve.wait_ge(logits_ps, n + 1)
                    dve.wait_ge(xn_hi_up, n + 1)
                    dve.wait_ge(xn_lo_up, n + 1)

                def routing(n, s):
                    tt = nc.vector.tensor_tensor
                    c = choice[:].rearrange("p (g e) -> p g e", e=GE)
                    gs = g_score[:].rearrange("p (j a) -> p j a", a=GROUPS)
                    other = gs.unsqueeze(2).broadcast_to([P, SUB, GROUPS, GROUPS])
                    own = gs.unsqueeze(3).broadcast_to([P, SUB, GROUPS, GROUPS])
                    before = g["before"][:].rearrange("p (j a c) -> p j a c", a=GROUPS, c=GROUPS)
                    norm3, rest3, raw3 = (b[:].rearrange("p (j e) -> p j e", e=E) for b in (w_norm, w_rest, w_raw))
                    inv3 = w_inv1[:].unsqueeze(2).broadcast_to([P, SUB, E])
                    if s == 0:
                        dve.wait_ge(logits_ps, n + 1)
                        link(nc.vector.tensor_scalar(zero_fix[:], misc_ps[:, 0:NE], 0.0, 1e-30, ALU.is_equal, ALU.mult), n, 1)
                    if s == 1:
                        nc.vector.tensor_add(logit[:], zero_fix[:], misc_ps[:, 0:NE]).then_inc(logits_taken, 1)
                    if s == 2:
                        dve.wait_ge(logits_taken, n + 1)
                        nc.vector.reciprocal(inv_logit[:], logit[:]).then_inc(inv_up, 1)
                    if s == 3:
                        dve.wait_ge(choice_up, n + 1)
                        tt(hi4[:], c[:, :, 0:4], c[:, :, 4:8], ALU.max)
                        link(tt(lo4[:], c[:, :, 0:4], c[:, :, 4:8], ALU.min), n, 2)
                    if s == 4:
                        tt(hi2[:], hi4[:, :, 0:2], hi4[:, :, 2:4], ALU.max)
                        tt(m2[:], hi4[:, :, 0:2], hi4[:, :, 2:4], ALU.min)
                        link(tt(n2[:], lo4[:, :, 0:2], lo4[:, :, 2:4], ALU.max), n, 3)
                    if s == 5:
                        tt(hi1[:], hi2[:, :, 0], hi2[:, :, 1], ALU.max)
                        tt(m1[:], hi2[:, :, 0], hi2[:, :, 1], ALU.min)
                        link(tt(lo2[:], m2[:], n2[:], ALU.max), n, 4)
                    if s == 6:
                        link(tt(n1[:], lo2[:, :, 0], lo2[:, :, 1], ALU.max), n, 5)
                    if s == 7:
                        link(tt(lo1[:], m1[:], n1[:], ALU.max), n, 6)
                    if s == 8:
                        link(tt(g_score[:], hi1[:], lo1[:], ALU.add), n, 7)
                    if s == 9:
                        tt(g_gt[:], other, own, ALU.is_gt)
                        link(tt(g_eq[:], other, own, ALU.is_equal), n, 8)
                    if s == 10:
                        link(tt(g_tie[:], g_eq[:], before, ALU.mult), n, 9)
                    if s == 11:
                        link(tt(g_beaten[:], g_gt[:], g_tie[:], ALU.add), n, 10)
                    if s == 12:
                        link(nc.vector.reduce_sum(g_count[:], g_beaten[:].rearrange("p j a c -> p (j a) c"), AX.X), n, 11)
                    if s == 13:
                        nc.vector.tensor_scalar(g_keep[:], g_count[:], float(KEEP_GROUPS), None, ALU.is_lt).then_inc(keep_up, 1)
                    if s == 14:
                        dve.wait_ge(masked_up, n + 1)
                    if s == 15:
                        for j in range(SUB):
                            last = nc.vector.max(top8[:, j, :], masked[:, j * E:(j + 1) * E])
                        link(last, n, 12)
                    if s == 16:
                        for j in range(SUB):
                            last = nc.vector.match_replace(left[:, j * E:(j + 1) * E], top8[:, j, :],
                                                           masked[:, j * E:(j + 1) * E], NEG)
                        link(last, n, 13)
                    if s == 17:
                        link(tt(picked[:], left[:], masked[:], ALU.not_equal), n, 14)
                    if s == 18:
                        link(nc.vector.tensor_mul(w_raw[:], picked[:], score[:]), n, 15)
                    if s == 19:
                        link(nc.vector.reduce_sum(w_sum[:], raw3, AX.X), n, 16)
                    if s == 20:
                        link(nc.vector.tensor_scalar_add(w_sum1[:], w_sum[:], 1e-20), n, 17)
                    if s == 21:
                        link(nc.vector.reciprocal(w_inv[:], w_sum1[:]), n, 18)
                    if s == 22:
                        nc.vector.tensor_scalar_mul(w_inv1[:], w_inv[:], SCALING).then_inc(raw_up, 1)
                    if s == 23:
                        dve.wait_ge(raw_up, n + 1)
                        dve.wait_ge(w_t_in_ps, n)
                        tt(norm3, raw3, inv3, ALU.mult)
                        link(tt(w_split[:, :, 0:E], raw3, inv3, ALU.mult), n, 19)
                    if s == 24:
                        tt(rest3, norm3, w_split[:, :, 0:E], ALU.subtract)
                        link(tt(w_split[:, :, E:2 * E], norm3, w_split[:, :, 0:E], ALU.subtract), n, 20)
                    if s == 25:
                        tt(w_split[:, :, 2 * E:], rest3, w_split[:, :, E:2 * E], ALU.subtract).then_inc(split_up, 1)

                PLAN = {0: (0, 1, 2), 4: (3, 4, 5), 5: (6, 7, 8), 6: (9, 10, 11, 12), 7: (13,), 9: (14, 15),
                        10: (16, 17, 18), 11: (19, 20, 21), 13: (22, 23, 24), 14: (25,)}

                def turn(it, par):
                    i = it * 2 + par
                    for p in range(STEPS):
                        k = i * STEPS + p
                        b = (STEPS * par + p) % 2
                        h = hidden[b]
                        dve.wait_ge(silu_done, k + 2 + 1)
                        dve.wait_ge(up_up, k + 1)
                        dve.wait_ge(hi_up, k + 1)
                        dve.wait_ge(lo_up, k + 1)
                        if p == 0:
                            nc.vector.tensor_mul(h[:], act_g[b][:], up_ps[b][:]).then_inc(hidden_up, 1)
                        else:
                            nc.vector.tensor_mul(prod[b][:], act_g[b][:], up_ps[b][:]).then_inc(up_used, 1)
                            for s in PLAN.get(p, ())[:1]:
                                routing(i + 1, s)
                            dve.wait_ge(up_used, i * PAIRS + p + 2)
                            dve.wait_ge(wbc_up, i * PAIRS + p)
                            nc.vector.tensor_mul(h[:], prod[b][:], wbc_ps[p % 2][:]).then_inc(hidden_up, 1)
                        if p == 1:
                            dve.wait_ge(down_done, k + 2)
                            nc.vector.scalar_tensor_tensor(tile(x, i), out_ps[:], 0.5, tile(x, i),
                                                           ALU.mult, ALU.add).then_inc(tile_done, 1)
                        if post and p == 4:
                            take_var(post_no(i))
                        if post and p == 8:
                            dve.wait_ge(xn_stored[par], 16 * it + 1)
                            scale(post_no(i), xn_out[par][:])
                        if p == 12:
                            take_var(pre_no(i))
                        if p == 15:
                            xn_free(i + 1)
                            scale(pre_no(i), xn[:])
                        for s in PLAN.get(p, ())[0 if p == 0 else 1:]:
                            routing(i + 1, s)

                nc.vector.memset(hi1[:], 0.0).then_inc(up_used, 1)
                nc.vector.memset(lo1[:], 0.0).then_inc(hidden_up, 1)
                nc.vector.memset(out_ps[:], 0.0).then_inc(init, 1)
                if x_dram is not None:
                    nc.vector.memset(tile(x, 0), 0.0).then_inc(init, 1)
                dve.wait_ge(g["consts"], g["n_consts"])
                def weights_low(c):
                    w = (w_gate, w_up, w_down)[c // 2]
                    at = slice(c % 2 * PIECE, (c % 2 + 1) * PIECE)
                    dve.wait_ge(staged[c], 16)
                    dve.wait_ge(piece_hi, c + 1)
                    nc.vector.tensor_sub(w[1][:, at], stage[c][:], w[0][:, at].bitcast(F32)).then_inc(piece_lo, 1)

                def routing_steps(first, last):
                    for s in range(first, last + 1):
                        routing(0, s)

                take_var(0)
                weights_low(0)
                scale(0, xn[:])
                weights_low(1)
                routing_steps(0, 2)
                routing_steps(3, 13)
                take_var(1)
                routing_steps(14, 17)
                weights_low(2)
                routing_steps(18, 21)
                xn_free(0)
                scale(1, xn[:])
                routing_steps(22, 25)
                weights_low(3)
                weights_low(4)
                weights_low(5)
                with dve.Fori(0, NT // 2) as it:
                    for par in range(2):
                        turn(it, par)
                dve.wait_ge(down_done, NT * STEPS + 2 + 1)
                nc.vector.scalar_tensor_tensor(tile(x, NT), out_ps[:], 0.5, tile(x, NT),
                                               ALU.mult, ALU.add).then_inc(tile_done, 1)
                if post:
                    take_var(post_no(NT))
                    dve.wait_ge(xn_stored[0], 16 * (NT // 2) + 1)
                    scale(post_no(NT), xn_out[0][:])



def attention_phase(nc, g, dram):
    xn_dram = g["xn_dram"]
    x = g["x"]
    KB = SUB
    P_AT = [P * j * (j + 1) // 2 for j in range(KB)]
    P_COLS = P * KB * (KB + 1) // 2
    BANKS = [(0,), (1, 3), (2,)]
    T_AT = {0: 0, 1: T, 3: T + 3 * P, 2: 2 * T}
    BANK_COLS = [(0, T), (T, 2 * T), (2 * T, 2 * T + 2 * P)]
    S_GROUPS = [(3,), (2,), (1, 0)]
    S_AT = {3: 0, 2: 0, 1: 0, 0: 2 * P}
    LEAD = 5
    NH = SPLIT * HEAD_ROWS
    CHUNK_STEPS = (0, 1, 2, 3, 12, 13, 14, 15)
    with ExitStack() as ctx:
        def sb(name, shape, dt=F32):
            return ctx.enter_context(nc.sbuf_tensor(f"a_{name}", shape, dt))

        def sem(name):
            return ctx.enter_context(nc.semaphore(f"a_{name}"))

        def pb(name):
            return ctx.enter_context(nc.psum_tensor(f"a_{name}", [P, T], F32))

        rot = [sb("rot_q", [P, 2 * T]), sb("rot_k", [P, 2 * T])]
        w_qkv = [sb(f"w_qkv_{p}", [P, 3 * HEADS * D], F32R) for p in ("hi", "lo")]
        w_out = [sb(f"w_out_{p}", [P, HP * P], F32R) for p in ("hi", "lo")]
        x_in = sb("x_in", [P, T])
        xc = [sb(f"xc_{p}", [P, T], F32R) for p in ("hi", "lo")]
        by_cos, swapped = ([sb(f"{n}{i}", [P, T]) for i in range(2)] for n in ("by_cos", "swapped"))
        rotated = sb("rotated", [P, T])
        qk = [[[sb(f"{kind}{i}_{p}", [P, T], F32R) for p in ("hi", "lo")] for i in range(2)] for kind in "qk"]
        v = sb("v", [P, KB, HP, 4, D], F32R)
        e_rows = [sb(f"e_rows{i}", [P, P_COLS]) for i in range(2)]
        e_cols = [[sb(f"e_cols{i}_{p}", [P, P_COLS], F32R) for p in ("hi", "lo")] for i in range(2)]
        neg_max = [sb(f"neg_max{i}", [P, KB]) for i in range(2)]
        row_sum = sb("row_sum", [P, KB, HEADS])
        inv_sum, inv_rest = sb("inv_sum", [P, KB, HEADS]), sb("inv_rest", [P, KB, HEADS])
        inv_split = sb("inv_split", [P, KB, NH], BF16)
        inv_t = sb("inv_t", [NH, T], BF16)
        o_raw = sb("o_raw", [P, HP, T])
        o_rest = sb("o_rest", [P, T])
        o_one = sb("o_one", [P, T])
        o_parts = [sb(f"o_{p}", [P, T], F32R) for p in ("hi", "lo")]

        s_banks = [pb(f"s{i}") for i in range(2)]
        t_banks = [pb(f"t{i}") for i in range(2)]
        o_ps, out_ps, qk_ps, misc_ps = pb("o"), pb("out"), pb("qk"), pb("misc")
        inv_t_ps = misc_ps[0:NH, :].bitcast(BF16)

        WP = HEADS * D
        W_PIECES = [("w_qkv", 0, 0), ("w_qkv", WP, 1), ("w_qkv", 2 * WP, 2), ("w_out", 0, 3)]
        w_in = [sem(f"w_in{i}") for i in range(len(W_PIECES))]
        rot_in, x_loaded, init = sem("rot_in"), sem("x_loaded"), sem("init")
        w_hi_up, w_lo_up = sem("w_hi_up"), sem("w_lo_up")
        xc_hi_up, xc_lo_up = sem("xc_hi_up"), sem("xc_lo_up")
        proj_ps, proj_taken = sem("proj_ps"), sem("proj_taken")
        sin_up, rotated_up = sem("sin_up"), sem("rotated_up")
        qk_hi_up, qk_lo_up = sem("qk_hi_up"), sem("qk_lo_up")
        v_ps, v_hi_up, v_lo_up = sem("v_ps"), sem("v_hi_up"), sem("v_lo_up")
        s_ps, max_up, exp_up = sem("s_ps"), sem("max_up"), sem("exp_up")
        t_ps, t_hi_up, t_lo_up = sem("t_ps"), sem("t_hi_up"), sem("t_lo_up")
        av_ps, o_up, o_sum_up = sem("av_ps"), sem("o_up"), sem("o_sum_up")
        inv_up, inv_split_up, inv_chain = sem("inv_up"), sem("inv_split_up"), sem("inv_chain")
        inv_t_in_ps, inv_t_up = sem("inv_t_in_ps"), sem("inv_t_up")
        bc_ps, one_up, one_hi_up, one_lo_up = sem("bc_ps"), sem("one_up"), sem("one_hi_up"), sem("one_lo_up")
        out_mm, added = sem("out_mm"), sem("added")

        start_at_1 = (av_ps, one_up, out_mm, one_lo_up, inv_t_in_ps, added)

        def chunk(b, h):
            return (8 * b + 4 + h, h, 1) if h < 4 else (8 * (b + 1) + h - 12, h - 12, 0)

        def before(b, h):
            return chunk(b, h - 1) if h else (8 * b + 3, 3, 0)

        def s_bank(h, group):
            return s_banks[(3 * h + group) % 2]

        def t_bank(h, bank):
            return t_banks[(3 * h + bank) % 2]

        def staged_w(place):
            return o_raw[:, 2 * place:2 * place + 2, :].rearrange("p a t -> p (a t)")

        def w_piece(i, part):
            src, at, _ = W_PIECES[i]
            return (w_qkv if src == "w_qkv" else w_out)[part][:, at:at + WP]

        def v_part(part, block, half):
            slots = slice(0, 4, 3) if part == 0 else slice(1, 3)
            return v[:, block, half * HP // 2:(half + 1) * HP // 2, slots, :]

        def by_head(bank):
            return bank[:].rearrange("p (a e d) -> p a e d", e=2, d=D)

        last_bank, last_one, last_parts = (misc_ps, qk_ps), (o_one, rotated), (o_parts, xc)

        with nc.Block() as block:

            @block.sync
            def _(sp):
                sp.dma_start(x_in[:], xn_dram[:, T:2 * T]).then_inc(x_loaded, 16)
                for i, (src, at, place) in enumerate(W_PIECES):
                    sp.dma_start(staged_w(place), dram[src][:, at:at + WP]).then_inc(w_in[i], 16)
                    if i == 0:
                        sp.dma_start(rot[0][:], dram["rot_q"]).then_inc(rot_in, 16)
                        sp.dma_start(rot[1][:], dram["rot_k"]).then_inc(rot_in, 16)
                with sp.Fori(0, NT - 1) as b:
                    sp.wait_ge(xc_lo_up, b + 1)
                    sp.dma_start(x_in[:], xn_dram[:, bass.ds(b * T + 2 * T, T)]).then_inc(x_loaded, 16)
                sp.wait_ge(xc_lo_up, NT)
                sp.dma_start(x_in[:], xn_dram[:, T:2 * T]).then_inc(x_loaded, 16)

            @block.tensor
            def _(pe):
                def mm3(out, w, x, start=True, stop=True):
                    nc.tensor.matmul(out, w[0], x[0], start=start, stop=False, skip_group_check=True)
                    nc.tensor.matmul(out, w[0], x[1], start=False, stop=False, skip_group_check=True)
                    return nc.tensor.matmul(out, w[1], x[0], start=False, stop=stop, skip_group_check=True)

                def project(r, kind, hp):
                    at = kind * HEADS * D + hp * P
                    mm3(qk_ps[:], [w[:, at:at + P] for w in w_qkv], (xc[0][:], xc[1][:])).then_inc(proj_ps, 1)

                def values(block, half):
                    at = 2 * HEADS * D + half * T
                    cols = slice(block * P, (block + 1) * P)
                    mm3(misc_ps[:], [p[:, cols] for p in xc], [w[:, at:at + T] for w in w_qkv]).then_inc(v_ps, 1)

                def scores(n, h, group):
                    e, par = h % 2, h // 2 % 2
                    rows = slice(D * e, D * e + D)
                    for j in S_GROUPS[group]:
                        out = s_bank(h, group)[:, S_AT[j]:S_AT[j] + (j + 1) * P]
                        mm3(out, [p[rows, j * P:(j + 1) * P] for p in qk[0][par]],
                            [p[rows, 0:(j + 1) * P] for p in qk[1][par]],
                            start=(j == S_GROUPS[group][0]), stop=False)
                    diagonal = S_AT[S_GROUPS[group][0]] + S_GROUPS[group][0] * P
                    width = P * len(S_GROUPS[group])
                    nc.tensor.matmul(s_bank(h, group)[:, diagonal:diagonal + width], g["ident16"][:],
                                     g["mask16"][:, 0:width], start=False, stop=True,
                                     skip_group_check=True).then_inc(s_ps, 1)

                def transposes(n, h, bank):
                    if n is not None:
                        pe.wait_ge(t_lo_up, 3 * n + bank - 1)
                    elif bank == 2:
                        pe.wait_ge(t_lo_up, 1)
                    for k in BANKS[bank]:
                        for j in range(k, KB):
                            at = T_AT[k] - bank * T + (j - k) * P
                            last = nc.tensor.transpose(t_bank(h, bank)[:, at:at + P],
                                                       e_rows[h % 2][:, P_AT[j] + k * P:P_AT[j] + (k + 1) * P],
                                                       g["ident"][:])
                    last.then_inc(t_ps, 1)

                def attend(n, h, bank):
                    e = h % 2
                    pe.wait_ge(t_lo_up, 3 * n + bank + 1)
                    for k in BANKS[bank]:
                        cols = slice(T_AT[k], T_AT[k] + T - k * P)
                        both = v[:, k, h // 2, 2 * e:2 * e + 2, :].rearrange("p a d -> p (a d)")
                        nc.tensor.matmul(o_ps[:, k * P:T], both, e_cols[e][0][:, cols],
                                         start=(k == 0), stop=False, skip_group_check=True)
                        last = nc.tensor.matmul(o_ps[:, k * P:T], both, e_cols[e][1][:, cols],
                                                start=False, stop=(k == 2), skip_group_check=True)
                    if bank == 2:
                        last.then_inc(av_ps, 1)

                def inverse_t():
                    for j in range(KB):
                        last = nc.tensor.transpose(inv_t_ps[:, j * P:(j + 1) * P], inv_split[:, j, :], g["ident16"][:])
                    last.then_inc(inv_t_in_ps, 1)

                def broadcast(p, bank=misc_ps):
                    nc.tensor.matmul(bank[:], g["sel_head"][:, p * P:(p + 1) * P], inv_t[:],
                                     start=True, stop=True).then_inc(bc_ps, 1)

                def out_project(p, parts=o_parts):
                    mm3(out_ps[:], [w[:, p * P:(p + 1) * P] for w in w_out], (parts[0][:], parts[1][:]),
                        start=(p == 0), stop=(p == HP - 1)).then_inc(out_mm, 1)

                pe.wait_ge(xc_hi_up, 1)
                pe.wait_ge(xc_lo_up, 1)
                for r in range(LEAD):
                    pe.wait_ge(w_hi_up, min(r + 1, 2))
                    pe.wait_ge(w_lo_up, min(r + 1, 2))
                    if r:
                        pe.wait_ge(proj_taken, r)
                    project(r, r % 2, r // 2)
                    c = r - 1
                    if c >= 0:
                        pe.wait_ge(w_hi_up, 3)
                        pe.wait_ge(w_lo_up, 3)
                        if c:
                            pe.wait_ge(v_lo_up, c)
                        values(c, 0)
                    if r == 2:
                        pe.wait_ge(qk_hi_up, 2)
                        pe.wait_ge(qk_lo_up, 2)
                        scores(0, 0, 0)
                        scores(0, 0, 1)
                    if r == 3:
                        pe.wait_ge(exp_up, 1)
                        scores(0, 0, 2)
                pe.wait_ge(exp_up, 2)
                scores(1, 1, 0)
                pe.wait_ge(exp_up, 3)
                transposes(None, 0, 0)
                scores(1, 1, 1)
                transposes(None, 0, 1)
                pe.wait_ge(exp_up, 4)
                scores(1, 1, 2)
                transposes(None, 0, 2)
                pe.wait_ge(w_hi_up, 4)
                pe.wait_ge(w_lo_up, 4)
                pe.wait_ge(init, 2)
                with pe.Fori(0, NT) as b:
                    for h in range(HEADS):
                        n, hp, e = b * HEADS + h, h // 2, h % 2
                        h1, h2 = (h + 1) % HEADS, (h + 2) % HEADS
                        if e == 0:
                            pe.wait_ge(qk_hi_up, n + 4)
                            pe.wait_ge(qk_lo_up, n + 4)
                        pe.wait_ge(exp_up, 3 * n + 5)
                        scores(n + 2, h2, 0)
                        if h == HEADS - LEAD:
                            pe.wait_ge(xc_hi_up, b + 2)
                            pe.wait_ge(xc_lo_up, b + 2)
                        pe.wait_ge(proj_taken, n + LEAD)
                        project(n + LEAD, 1 - e, (h + LEAD) // 2 % HP)
                        pe.wait_ge(exp_up, 3 * n + 6)
                        transposes(n + 1, h1, 0)
                        pe.wait_ge(exp_up, 3 * n + 6)
                        scores(n + 2, h2, 1)
                        if e == 0:
                            if h == 0 or h - 1 in CHUNK_STEPS:
                                pe.wait_ge(v_lo_up, before(b, h)[0] + 1)
                            else:
                                pe.wait_ge(one_up, 8 * b + hp + 1)
                            if h == 0:
                                pe.wait_ge(inv_t_up, b + 1)
                            broadcast(hp)
                        if h == HEADS - 1:
                            pe.wait_ge(v_lo_up, before(b, h)[0] + 1)
                            pe.wait_ge(inv_split_up, b + 1)
                            inverse_t()
                        if h == 0:
                            pe.wait_ge(v_lo_up, 8 * b + 4)
                        if h == 8:
                            pe.wait_ge(v_lo_up, 8 * b + 8)
                        pe.wait_ge(o_up, n + 1)
                        attend(n, h, 0)
                        attend(n, h, 1)
                        transposes(n + 1, h1, 1)
                        pe.wait_ge(exp_up, 3 * n + 7)
                        scores(n + 2, h2, 2)
                        transposes(n + 1, h1, 2)
                        if e == 1:
                            pe.wait_ge(one_hi_up, 8 * b + hp + 1)
                            pe.wait_ge(one_lo_up, 8 * b + hp + 2)
                            if hp == 0:
                                pe.wait_ge(added, b + 1)
                            out_project(hp)
                        attend(n, h, 2)
                        if h in CHUNK_STEPS:
                            if e == 0:
                                pe.wait_ge(one_up, 8 * b + hp + 2)
                            elif h == HEADS - 1:
                                pe.wait_ge(inv_t_up, b + 2)
                            else:
                                pe.wait_ge(v_lo_up, before(b, h)[0] + 1)
                            _, blk, half = chunk(b, h)
                            values(blk, half)

                pe.wait_ge(inv_t_up, NT + 1)
                broadcast(0)
                pe.wait_ge(proj_taken, NT * HEADS + LEAD)
                broadcast(1, last_bank[1])
                for p in range(HP):
                    if p + 2 < HP:
                        pe.wait_ge(one_up, 8 * NT + p + 2)
                        broadcast(p + 2, last_bank[p % 2])
                    pe.wait_ge(one_hi_up, 8 * NT + p + 1)
                    pe.wait_ge(one_lo_up, 8 * NT + p + 2)
                    if p == 0:
                        pe.wait_ge(added, NT + 1)
                    out_project(p, last_parts[p % 2])

            @block.scalar
            def _(act):
                copy = nc.scalar.copy

                def qk_high(r, kind, par):
                    act.wait_ge(rotated_up, r + 1)
                    copy(qk[kind][par][0][:], rotated[:]).then_inc(qk_hi_up, 1)

                def exps(n, h, group):
                    act.wait_ge(max_up, 3 * n + group + 1)
                    for j in S_GROUPS[group]:
                        last = nc.scalar.activation(e_rows[h % 2][:, P_AT[j]:P_AT[j] + (j + 1) * P],
                                                    s_bank(h, group)[:, S_AT[j]:S_AT[j] + (j + 1) * P], ACT.Exp,
                                                    bias=neg_max[h % 2][:, j:j + 1], accum_out=row_sum[:, j, h:h + 1])
                    last.then_inc(exp_up, 1)

                def e_high(n, h, bank):
                    act.wait_ge(t_ps, 3 * n + bank + 1)
                    lo, hi = BANK_COLS[bank]
                    copy(e_cols[h % 2][0][:, lo:hi], t_bank(h, bank)[:, 0:hi - lo]).then_inc(t_hi_up, 1)

                def v_high(c, blk, half):
                    act.wait_ge(v_ps, c + 1)
                    copy(v_part(0, blk, half), by_head(misc_ps)).then_inc(v_hi_up, 1)

                def xc_high(b):
                    act.wait_ge(x_loaded, 16 * (b + 1))
                    copy(xc[0][:], x_in[:]).then_inc(xc_hi_up, 1)

                def take_o(n, h, divided, summed):
                    act.wait_ge(av_ps, n + 1)
                    act.wait_ge(one_up, divided + 1)
                    e = h % 2
                    rows, others = slice(e * D, e * D + D), slice((1 - e) * D, (2 - e) * D)
                    copy(o_raw[rows, h // 2, :], o_ps[rows, :])
                    if summed is not None:
                        act.wait_ge(o_sum_up, summed)
                    copy(o_rest[rows, :], o_ps[others, :]).then_inc(o_up, 1)

                def one_high(m):
                    act.wait_ge(one_up, m + 2)
                    act.wait_ge(out_mm, m + 1)
                    copy(o_parts[0][:], o_one[:]).then_inc(one_hi_up, 1)

                def take_inverse(b):
                    act.wait_ge(inv_t_in_ps, b + 1)
                    copy(inv_t[:], inv_t_ps[:, 0:T]).then_inc(inv_t_up, 1)

                act.wait_ge(x_loaded, 16)
                nc.scalar.activation(neg_max[0][:, 0:1], x_in[:, 0:1], ACT.Exp)
                xc_high(0)
                for i in range(len(W_PIECES)):
                    act.wait_ge(w_in[i], 16)
                    copy(w_piece(i, 0), staged_w(W_PIECES[i][2])).then_inc(w_hi_up, 1)
                for r in range(LEAD - 1):
                    qk_high(r, r % 2, r // 2 % 2)
                    if r < 3:
                        v_high(r, r, 0)
                    if r == 1:
                        exps(0, 0, 0)
                        exps(0, 0, 1)
                    if r == 2:
                        exps(0, 0, 2)
                for i in range(3):
                    exps(1, 1, i)
                    e_high(0, 0, i)
                act.wait_ge(init, 2)
                act.wait_ge(w_lo_up, 4)
                with act.Fori(0, NT) as b:
                    for h in range(HEADS):
                        n, hp, e = b * HEADS + h, h // 2, h % 2
                        h1, h2 = (h + 1) % HEADS, (h + 2) % HEADS
                        if h == 0 or h - 1 in CHUNK_STEPS:
                            v_high(*before(b, h))
                        take_o(n, (h - 1) % HEADS, 8 * b + hp + e, 8 * b + hp + 1 if e else None)
                        if h == HEADS - LEAD - 1:
                            act.wait_ge(proj_ps, n + LEAD + 1)
                            xc_high(b + 1)
                        if e == 1:
                            one_high(8 * b + hp)
                        act.wait_ge(av_ps, n + 1)
                        e_high(n + 1, h1, 0)
                        if h == HEADS - 2:
                            act.wait_ge(inv_up, b + 1)
                        act.wait_ge(t_ps, 3 * n + 3)
                        exps(n + 2, h2, 0)
                        act.wait_ge(s_ps, 3 * n + 6)
                        qk_high(n + LEAD - 1, e, (h + LEAD - 1) // 2 % 2)
                        e_high(n + 1, h1, 1)
                        if h == HEADS - 1:
                            take_inverse(b + 1)
                        exps(n + 2, h2, 1)
                        e_high(n + 1, h1, 2)
                        exps(n + 2, h2, 2)
                take_o(NT * HEADS, HEADS - 1, 8 * NT, None)
                for p in range(HP):
                    act.wait_ge(one_up, 8 * NT + p + 2)
                    if p == 1:
                        act.wait_ge(v_ps, 8 * NT + 4)
                    else:
                        act.wait_ge(out_mm, 8 * NT + max(p - 1, 0) + 1)
                    copy(last_parts[p % 2][0][:], last_one[p % 2][:]).then_inc(one_hi_up, 1)

            @block.gpsimd
            def _(pool):
                tt = nc.gpsimd.tensor_tensor

                def rotate(r, kind, lows=0):
                    pool.wait_ge(proj_taken, r + 1)
                    tt(swapped[kind][:], swapped[kind][:], rot[kind][:, T:], ALU.mult).then_inc(sin_up, 1)
                    pool.wait_ge(sin_up, r + 1)
                    pool.wait_ge(qk_hi_up, r)
                    if lows:
                        pool.wait_ge(qk_lo_up, lows)
                    tt(rotated[:], by_cos[kind][:], swapped[kind][:], ALU.add).then_inc(rotated_up, 1)

                def qk_low(r, kind, par):
                    pool.wait_ge(qk_hi_up, r + 1)
                    hi, lo = qk[kind][par]
                    tt(lo[:], rotated[:], hi[:].bitcast(F32), ALU.subtract).then_inc(qk_lo_up, 1)

                def sum_parts(p, taken):
                    pool.wait_ge(o_up, taken)
                    tt(o_raw[:, p, :], o_raw[:, p, :], o_rest[:], ALU.add).then_inc(o_sum_up, 1)

                def one_low(m, one=o_one, parts=o_parts):
                    pool.wait_ge(one_hi_up, m + 1)
                    tt(parts[1][:], one[:], parts[0][:].bitcast(F32), ALU.subtract).then_inc(one_lo_up, 1)

                def xc_low(b):
                    pool.wait_ge(xc_hi_up, b + 1)
                    tt(xc[1][:], x_in[:], xc[0][:].bitcast(F32), ALU.subtract).then_inc(xc_lo_up, 1)

                for count in start_at_1:
                    nc.gpsimd.sem_inc(count, 1)
                nc.gpsimd.memset(inv_t[:], 0.0).then_inc(inv_t_up, 1)
                xc_low(0)
                nc.gpsimd.memset(o_rest[:], 0.0).then_inc(init, 1)
                pool.wait_ge(rot_in, 32)
                for r in range(LEAD):
                    rotate(r, r % 2, lows=r)
                with pool.Fori(0, NT) as b:
                    for h in range(HEADS):
                        n, hp, e = b * HEADS + h, h // 2, h % 2
                        if e == 0:
                            sum_parts((hp - 1) % HP, n + 1)
                        if e == 1:
                            one_low(8 * b + hp)
                        if h == HEADS - LEAD - 1:
                            xc_low(b + 1)
                        qk_low(n + LEAD - 1, e, (h + LEAD - 1) // 2 % 2)
                        rotate(n + LEAD, 1 - e)
                sum_parts(HP - 1, NT * HEADS + 1)
                for p in range(HP):
                    one_low(8 * NT + p, last_one[p % 2], last_parts[p % 2])

            @block.vector
            def _(dve):
                def take_projection(r, kind):
                    dve.wait_ge(proj_ps, r + 1)
                    if not isinstance(r, int) or r > 1:
                        dve.wait_ge(rotated_up, r - 1)
                    nc.vector.tensor_mul(by_cos[kind][:], qk_ps[:], rot[kind][:, 0:T])
                    nc.vector.stream_shuffle(swapped[kind][:], qk_ps[:], [i ^ 1 for i in range(32)]).then_inc(proj_taken, 1)

                def maxima(n, h, group):
                    dve.wait_ge(s_ps, 3 * n + group + 1)
                    for j in S_GROUPS[group]:
                        last = nc.vector.tensor_reduce(neg_max[h % 2][:, j:j + 1],
                                                       s_bank(h, group)[:, S_AT[j]:S_AT[j] + (j + 1) * P],
                                                       AX.X, ALU.max, negate=True)
                    last.then_inc(max_up, 1)

                def e_low(n, h, bank):
                    dve.wait_ge(t_hi_up, 3 * n + bank + 1)
                    lo, hi = BANK_COLS[bank]
                    nc.vector.tensor_tensor(e_cols[h % 2][1][:, lo:hi], t_bank(h, bank)[:, 0:hi - lo],
                                            e_cols[h % 2][0][:, lo:hi].bitcast(F32), ALU.subtract).then_inc(t_lo_up, 1)

                def split_inverses(b, step):
                    first, second, third = (inv_split[:, :, i * HEAD_ROWS:i * HEAD_ROWS + HEADS] for i in range(SPLIT))
                    if step == 0:
                        dve.wait_ge(inv_up, b + 1)
                        dve.wait_ge(inv_t_in_ps, b + 1)
                        dve.wait_ge(inv_chain, 2 * b + 1)
                        nc.vector.tensor_copy(first, inv_sum[:]).then_inc(inv_chain, 1)
                    if step == 1:
                        dve.wait_ge(inv_chain, 2 * b + 2)
                        nc.vector.tensor_sub(inv_rest[:], inv_sum[:], first)
                        nc.vector.tensor_sub(second, inv_sum[:], first).then_inc(inv_chain, 1)
                    if step == 2:
                        dve.wait_ge(inv_chain, 2 * b + 3)
                        nc.vector.tensor_sub(third, inv_rest[:], second).then_inc(inv_split_up, 1)

                def v_low(c, blk, half):
                    dve.wait_ge(v_hi_up, c + 1)
                    nc.vector.tensor_tensor(v_part(1, blk, half), by_head(misc_ps), v_part(0, blk, half).bitcast(F32),
                                            ALU.subtract).then_inc(v_lo_up, 1)

                def divide(m, p, taken):
                    dve.wait_ge(bc_ps, m + 1)
                    dve.wait_ge(one_lo_up, m + 1)
                    dve.wait_ge(o_sum_up, taken)
                    nc.vector.tensor_mul(o_one[:], o_raw[:, p, :], misc_ps[:]).then_inc(one_up, 1)

                def add_result(b, count):
                    dve.wait_ge(out_mm, count + 1)
                    nc.vector.tensor_add(tile(x, b), tile(x, b), out_ps[:]).then_inc(added, 1)

                def w_low(i):
                    dve.wait_ge(w_in[i], 16)
                    dve.wait_ge(w_hi_up, i + 1)
                    nc.vector.tensor_sub(w_piece(i, 1), staged_w(W_PIECES[i][2]), w_piece(i, 0).bitcast(F32)).then_inc(w_lo_up, 1)

                def qk_low_first(r, kind, par):
                    dve.wait_ge(qk_hi_up, r + 1)
                    hi, lo = qk[kind][par]
                    nc.vector.tensor_sub(lo[:], rotated[:], hi[:].bitcast(F32)).then_inc(qk_lo_up, 1)

                w_low(0)
                dve.wait_ge(rot_in, 32)
                take_projection(0, 0)
                w_low(1)
                w_low(2)
                for r in range(1, LEAD):
                    take_projection(r, r % 2)
                    qk_low_first(r - 1, (r - 1) % 2, (r - 1) // 2 % 2)
                    if r == 1:
                        w_low(3)
                        nc.vector.memset(o_ps[:], 0.0).then_inc(init, 1)
                        nc.vector.memset(inv_split[:], 0.0).then_inc(inv_chain, 1)
                    if r < 4:
                        v_low(r - 1, r - 1, 0)
                    if r == 2:
                        maxima(0, 0, 0)
                        maxima(0, 0, 1)
                    if r == 3:
                        maxima(0, 0, 2)
                for i in range(3):
                    maxima(1, 1, i)
                    e_low(0, 0, i)
                with dve.Fori(0, NT) as b:
                    for h in range(HEADS):
                        n, hp, e = b * HEADS + h, h // 2, h % 2
                        h1, h2 = (h + 1) % HEADS, (h + 2) % HEADS
                        maxima(n + 2, h2, 0)
                        if h == 0 or h - 1 in CHUNK_STEPS:
                            v_low(*before(b, h))
                        take_projection(n + LEAD, 1 - e)
                        if h == HEADS - 2:
                            dve.wait_ge(exp_up, 3 * n + 6)
                            nc.vector.reciprocal(inv_sum[:], row_sum[:]).then_inc(inv_up, 1)
                        e_low(n + 1, h1, 0)
                        if h == HEADS - 2:
                            split_inverses(b, 0)
                        maxima(n + 2, h2, 1)
                        if h == HEADS - 2:
                            split_inverses(b, 1)
                        if e == 0:
                            divide(8 * b + hp, hp, 8 * b + 1)
                        if h == HEADS - 2:
                            split_inverses(b, 2)
                        maxima(n + 2, h2, 2)
                        e_low(n + 1, h1, 1)
                        e_low(n + 1, h1, 2)
                        if h == HEADS - 1:
                            add_result(b, 8 * b + 8)
                dve.wait_ge(o_sum_up, 8 * NT + 1)
                for p in range(HP):
                    dve.wait_ge(bc_ps, 8 * NT + p + 1)
                    if p == 1:
                        dve.wait_ge(rotated_up, NT * HEADS + LEAD)
                    else:
                        dve.wait_ge(one_lo_up, 8 * NT + max(p - 1, 0) + 1)
                    nc.vector.tensor_mul(last_one[p % 2][:], o_raw[:, p, :], last_bank[p % 2][:]).then_inc(one_up, 1)
                add_result(NT, 8 * NT + 8)


def load_consts(nc, g, dram, ctx):
    def sb(name, shape, dt=F32):
        g[name] = ctx.enter_context(nc.sbuf_tensor(name, shape, dt))
        return g[name]

    f32 = {"ident": [P, P], "center": [P, P], "before": [P, SUB * GROUPS * GROUPS],
           "w_router": [P, E], "bias": [P, E]}
    for name, shape in f32.items():
        sb(name, shape)
    sb("ones", [P, P])
    sb("mean_col", [P, 1])
    sb("minus_half", [P, SUB])
    sb("ident16", [P, P], BF16)
    sb("mask16", [P, 2 * P], BF16)
    sb("sel_expert", [SPLIT * E, PAIRS * P], BF16)
    sb("sel_head", [SPLIT * HEAD_ROWS, HP * P], BF16)
    g["consts"] = ctx.enter_context(nc.semaphore("consts"))
    g["cast"] = ctx.enter_context(nc.semaphore("cast"))
    loads = len(f32)
    g["n_consts"] = 16 * loads + 3
    g["n_cast"] = 4
    with ExitStack() as tmp:
        stage = {n: tmp.enter_context(nc.sbuf_tensor(f"stage_{n}", s, F32)) for n, s in
                 (("mask", [P, P]), ("sel_expert", [SPLIT * E, PAIRS * P]), ("sel_head", [SPLIT * HEAD_ROWS, HP * P]))}
        staged = tmp.enter_context(nc.semaphore("staged"))
        with nc.Block() as block:

            @block.sync
            def _(sp):
                for name in f32:
                    src = dram[name]
                    if name == "bias":
                        src = src.broadcast_to([P, E])
                    sp.dma_start(g[name][:], src).then_inc(g["consts"], 16)
                for name, buf in stage.items():
                    sp.dma_start(buf[:], dram[name]).then_inc(staged, 16)

            @block.gpsimd
            def _(pool):
                nc.gpsimd.memset(g["ones"][:], 1.0).then_inc(g["consts"], 1)
                nc.gpsimd.memset(g["mean_col"][:], 1.0 / P).then_inc(g["consts"], 1)
                nc.gpsimd.memset(g["minus_half"][:], -0.5).then_inc(g["consts"], 1)

            @block.vector
            def _(dve):
                dve.wait_ge(g["consts"], g["n_consts"])
                nc.vector.tensor_copy(g["ident16"][:], g["ident"][:]).then_inc(g["cast"], 1)
                dve.wait_ge(staged, 16 * len(stage))
                nc.vector.tensor_copy(g["mask16"][:].rearrange("p (a t) -> p a t", a=2),
                                      stage["mask"][:].unsqueeze(1).broadcast_to([P, 2, P])).then_inc(g["cast"], 1)
                nc.vector.tensor_copy(g["sel_expert"][:], stage["sel_expert"][:]).then_inc(g["cast"], 1)
                nc.vector.tensor_copy(g["sel_head"][:], stage["sel_head"][:]).then_inc(g["cast"], 1)


def program(nc, dram, out):
    g = {}
    with ExitStack() as ctx:
        load_consts(nc, g, dram, ctx)
        g["x"] = ctx.enter_context(nc.sbuf_tensor("x", [P, SLOTS * T], F32))
        g["xn_dram"] = nc.dram_tensor("xn_scratch", [P, (NT + 1) * T], F32, kind="Internal").ap()
        ffn = (dram["w_gate"], dram["w_up"], dram["w_down"])
        ffn_phase(nc, "f1", g, ffn, dram["x"], None)
        attention_phase(nc, g, dram)
        ffn_phase(nc, "f2", g, ffn, None, out)


def layout(inputs):
    a = {k: np.asarray(v) for k, v in inputs.items()}
    f = {k[3:]: v for k, v in a.items()}
    x = f["attn_x"]
    lay = {"x": x.reshape(-1, P).T}
    for name, routed, shared in (("w_gate", "ffn_expert_gate", "ffn_shared_gate"), ("w_up", "ffn_expert_up", "ffn_shared_up")):
        lay[name] = np.concatenate([f[shared].T, f[routed].reshape(E * I, P).T], 1)
    down = f["ffn_expert_down"].transpose(0, 2, 1).reshape(PAIRS, P, P)
    lay["w_down"] = np.concatenate([f["ffn_shared_down"].T[None], down], 0).transpose(1, 0, 2).reshape(P, STEPS * P)
    lay["w_router"] = f["ffn_gate_w"].T
    lay["bias"] = f["ffn_gate_bias"].reshape(1, E)
    lay["w_qkv"] = f["attn_W_qkv"]
    lay["w_out"] = f["attn_W_out"].reshape(HP, P, P).transpose(1, 0, 2).reshape(P, HP * P)
    lay.update(constants())
    return {k: np.ascontiguousarray(v) for k, v in lay.items()}


def kernel(**inputs):
    import concourse.bacc as bacc
    from concourse.bass_utils import run_bass_kernel_spmd

    arrays = {f"in_{k}": v for k, v in layout(inputs).items()}
    nc = bacc.Bacc("TRN2", target_bir_lowering=False, num_devices=1)
    dram = {k[3:]: nc.dram_tensor(k, v.shape, mybir.dt.from_np(v.dtype), kind="ExternalInput").ap()
            for k, v in arrays.items()}
    out = nc.dram_tensor("out", [P, NT * T], F32, kind="ExternalOutput").ap()
    program(nc, dram, out)
    r = run_bass_kernel_spmd(nc, [arrays], core_ids=[0])
    return np.ascontiguousarray(r.results[0]["out"].T).reshape(NT, T, P)
```
